# Optimizing a Trainium2 kernel written in Bass

```python
import numpy as np
import jax
import jax.numpy as jnp

def _softmax(x, axis=-1):
    return jax.nn.softmax(x, axis=axis)

def _gelu(x):
    return jax.nn.gelu(x, approximate=True)

def _silu(x):
    return jax.nn.silu(x)

def _sigmoid(x):
    return jax.nn.sigmoid(x)

def _layernorm(x, axis=-1, eps=1e-05):
    m = jnp.mean(x, axis=axis, keepdims=True)
    v = jnp.var(x, axis=axis, keepdims=True)
    return (x - m) / jnp.sqrt(v + eps)

def _scatter_add(tgt, idx, src, axis=0):
    return tgt.at[idx].add(src)

def _segment_sum(src, seg, n):
    return jax.ops.segment_sum(src, seg, n)
kernel_name = 'mk_cond_resid_d2_seqx_r8_666c73'

def setup_inputs(seed: int=0):
    np.random.seed(seed)
    _w = jnp.asarray

    def _rec_inputs():
        import jax
        import jax.numpy as jnp
        _rk = jax.random.key(seed)
        x = -7.109e-05 + 0.9999 * jax.random.normal(jax.random.fold_in(_rk, 1), (128, 32, 512), jnp.float32)
        _lenS = 32 - jax.random.randint(jax.random.fold_in(_rk, 7), (128,), 0, max(1, 32 // 4) + 1, jnp.int32)
        _lenS2 = 32 - jax.random.randint(jax.random.fold_in(_rk, 8), (128,), 0, max(1, 32 // 4) + 1, jnp.int32)
        itok_B_0_31 = jax.random.randint(jax.random.fold_in(_rk, 11), (128,), 0, 32, jnp.int32)
        itok_B_0_23 = jax.random.randint(jax.random.fold_in(_rk, 12), (128,), 0, 24, jnp.int32)
        return (x, itok_B_0_31, itok_B_0_23)
    x, itok_B_0_31, itok_B_0_23 = _rec_inputs()

    def _L0_cond_setup():
        import jax, jax.numpy as jnp
        import numpy as np
        S, C, D = (32, 32, 32)
        B, T = (64, 512)
        key = jax.random.key(seed)
        k_x, k_w, k_s = jax.random.split(key, 3)
        x = jax.random.normal(k_x, (B, C, T), dtype=jnp.float32)
        subjects = jax.random.randint(k_s, (B,), 0, S, dtype=jnp.int64)
        std = float(np.sqrt(2.0 / (C + D)))
        weights = jax.random.normal(k_w, (S, C, D), dtype=jnp.float32) * std * (1.0 / np.sqrt(C))
        biases = jnp.zeros((S, 1, D), dtype=jnp.float32)
        return {'x': x, 'subjects': subjects, 'weights': weights, 'biases': biases}
    _L0_cond_all = _L0_cond_setup()
    _L0_cond_in = {k: v for k, v in _L0_cond_all.items() if k in ('weights', 'biases')}
    del _L0_cond_all

    def _L1_cond_setup():
        import jax, jax.numpy as jnp
        import numpy as np
        R = 16
        ALPHA = 32
        SCALING = ALPHA / R
        SLOTS = 32
        IN_F = 512
        OUT_F = 512
        B, T = (8, 128)
        key = jax.random.key(seed)
        k1, k2, k3, k4, k5, k6 = jax.random.split(key, 6)
        x = jax.random.normal(k1, (B, T, IN_F), dtype=jnp.float32)
        adapter_mapping = jax.random.randint(k2, (B,), 0, SLOTS, dtype=jnp.int32)
        W = jax.random.normal(k3, (OUT_F, IN_F), dtype=jnp.float32) * 0.02
        b = jax.random.normal(k4, (OUT_F,), dtype=jnp.float32) * 0.02
        lora_As = jax.random.normal(k5, (SLOTS, IN_F, R), dtype=jnp.float32) * 0.02
        lora_Bs = jax.random.normal(k6, (SLOTS, R, OUT_F), dtype=jnp.float32) * 0.02
        return {'x': x, 'adapter_mapping': adapter_mapping, 'W': W, 'b': b, 'lora_As': lora_As, 'lora_Bs': lora_Bs}
    _L1_cond_all = _L1_cond_setup()
    _L1_cond_in = {k: v for k, v in _L1_cond_all.items() if k in ('W', 'b', 'lora_As', 'lora_Bs')}
    del _L1_cond_all
    return {'x': x, 'itok_B_0_31': itok_B_0_31, 'itok_B_0_23': itok_B_0_23, 'L0_cond_weights': _L0_cond_in['weights'], 'L0_cond_biases': _L0_cond_in['biases'], 'L1_cond_W': _L1_cond_in['W'], 'L1_cond_b': _L1_cond_in['b'], 'L1_cond_lora_As': _L1_cond_in['lora_As'], 'L1_cond_lora_Bs': _L1_cond_in['lora_Bs']}

def reference(x, itok_B_0_31, itok_B_0_23, L0_cond_weights, L0_cond_biases, L1_cond_W, L1_cond_b, L1_cond_lora_As, L1_cond_lora_Bs):
    import jax
    import jax.numpy as jnp

    def _L0_cond_ref(x, subjects, weights, biases):
        import jax, jax.numpy as jnp
        import numpy as np
        S, C, D = (32, 32, 32)
        B, T = (64, 512)
        w = weights[subjects]
        b = biases[subjects]
        out = jnp.einsum('bct,bcd->bdt', x, w)
        return out + jnp.transpose(b, (0, 2, 1))

    def _L1_cond_ref(x, adapter_mapping, W, b, lora_As, lora_Bs):
        import jax, jax.numpy as jnp
        import numpy as np
        R = 16
        ALPHA = 32
        SCALING = ALPHA / R
        SLOTS = 32
        IN_F = 512
        OUT_F = 512
        B, T = (8, 128)
        base_out = jnp.einsum('bti,oi->bto', x, W) + b
        A = lora_As[adapter_mapping]
        Bm = lora_Bs[adapter_mapping]
        lora_h = jnp.einsum('bti,bir->btr', x, A)
        lora_out = jnp.einsum('btr,bro->bto', lora_h, Bm)
        return base_out + lora_out * SCALING
    x = x + _L0_cond_ref(x, itok_B_0_31, L0_cond_weights, L0_cond_biases)
    x = x + _L1_cond_ref(x, itok_B_0_23, L1_cond_W, L1_cond_b, L1_cond_lora_As, L1_cond_lora_Bs)
    return x

_drawn_inputs = setup_inputs


def setup_inputs(seed=0):
    import zlib

    import numpy as np

    out = dict(_drawn_inputs(seed))
    spreads = {'L0_cond_biases': (0.0, 0.1)}
    factors = {'L1_cond_b': 3.384}
    for name, (base, spread) in spreads.items():
        noise = np.random.default_rng([zlib.crc32(name.encode()), seed]).standard_normal(out[name].shape)
        drawn = base * np.exp(spread * noise) if base else spread * noise
        out[name] = jnp.asarray(drawn.astype(out[name].dtype))
    for name, factor in factors.items():
        out[name] = (out[name] * factor).astype(out[name].dtype)
    return out
```

```python
from contextlib import ExitStack

import concourse.bass as bass
from concourse import mybir

BATCH, ROWS, FEAT = 128, 32, 512
SLOTS, RANK = 32, 16
P = 128
PER_TILE = P // ROWS
TILES = BATCH // PER_TILE
CHUNKS = FEAT // P
HALF = FEAT // 2
HCOLS = PER_TILE * RANK
SCALING = 2.0
WROW = 2 * (HALF + HCOLS)


def build(nc, x, subj, slot, w0, b0, w1, b1, lora_a, lora_b, out):
    fp32 = mybir.dt.float32
    f32r = mybir.dt.float32r
    i32 = mybir.dt.int32
    ALU = mybir.AluOpType
    AX = mybir.AxisListType

    x_t = x.rearrange("(n b) c f -> n (b c) f", b=PER_TILE)
    out_t = out.rearrange("(n b) c f -> n (b c) f", b=PER_TILE)
    b_split = nc.dram_tensor("b_split", (SLOTS, 2 * RANK, FEAT), fp32, kind="Internal").ap()

    ctx = ExitStack()
    with ctx:
        def sb(name, shape, dt=fp32):
            return ctx.enter_context(nc.sbuf_tensor(name, shape, dt))

        def ps(name, shape):
            return ctx.enter_context(nc.psum_tensor(name, shape, fp32))

        def sem(name):
            return ctx.enter_context(nc.semaphore(name))

        index = sb("index", [1, 2, BATCH], i32)
        ident = sb("ident", [P, P])
        shifted = sb("shifted", [P, FEAT + CHUNKS])
        eye_rows = sb("eye_rows", [P, ROWS])
        lo_half = sb("lo_half", [P, 1])
        h_mask = sb("h_mask", [P, P])
        w_nat = sb("w_nat", [P, CHUNKS, FEAT])
        w_sum = sb("w_sum", [P, CHUNKS, FEAT])
        w_cat = sb("w_cat", [P, 2, CHUNKS, WROW], f32r)
        bias1 = sb("bias1", [P, FEAT])
        bias0 = sb("bias0", [P, SLOTS * ROWS])
        s_raw = sb("s_raw", [P, SLOTS, ROWS])
        s_sum = sb("s_sum", [P, SLOTS, ROWS])
        s_all = sb("s_all", [P, SLOTS, 2, ROWS], f32r)
        a_raw = sb("a_raw", [P, SLOTS, CHUNKS * RANK])
        a_all = sb("a_all", [P, SLOTS, 2, CHUNKS * RANK], f32r)
        b_raw = sb("b_raw", [P, SLOTS // 4, FEAT])
        b_hi = sb("b_hi", [P, SLOTS // 4, FEAT], f32r)
        b_cat = sb("b_cat", [P, SLOTS // 4, FEAT], f32r)

        x_raw = [sb(f"x_raw{u}", [P, FEAT]) for u in range(2)]
        x_hi = [sb(f"x_hi{u}", [P, FEAT], f32r) for u in range(2)]
        x_lo = [sb(f"x_lo{u}", [P, FEAT], f32r) for u in range(2)]
        w_blk = [sb(f"w_blk{u}", [P, 2, P], f32r) for u in range(2)]
        bias_t = [sb(f"bias_t{u}", [P, P]) for u in range(2)]
        b_t = [sb(f"b_t{u}", [P, FEAT], f32r) for u in range(2)]
        x2_hi = [sb(f"x2_hi{u}", [P, CHUNKS, P], f32r) for u in range(2)]
        x2_lo = [sb(f"x2_lo{u}", [P, CHUNKS, P], f32r) for u in range(2)]
        h_m = sb("h_m", [P, P])
        ht_hi = sb("ht_hi", [P, P], f32r)
        ht_lo = sb("ht_lo", [P, P], f32r)
        out_sb = [sb(f"out_sb{u}", [P, FEAT]) for u in range(2)]

        x2_ps = ps("x2_ps", [P, CHUNKS, P])
        ht_ps = ps("ht_ps", [P, P])
        out_ps = [ps(f"out_ps{u}", [P, 2, FEAT]) for u in range(2)]
        wt_ps = [out_ps[0][:, 0, :], out_ps[0][:, 1, :], out_ps[1][:, 0, :], out_ps[1][:, 1, :]]

        a_at = [HALF, 2 * HALF + HCOLS]
        second = [slice(HALF, 2 * HALF + HCOLS), slice(HALF + HCOLS, WROW)]
        h_at = [0, HALF]
        o_at = [HCOLS, 0]

        index_in, w_in, bias_in, s_in, a_in, b_in = (sem(n) for n in (
            "index_in", "w_in", "bias_in", "s_in", "a_in", "b_in"))
        x_in = [sem(f"x_in{u}") for u in range(2)]
        b_got = [sem(f"b_got{u}") for u in range(2)]
        stored = [sem(f"stored{u}") for u in range(2)]
        consts, blanks, masks = sem("consts"), sem("blanks"), sem("masks")
        wt_done, w_summed, w_hi_done, w_lo_done = (sem(n) for n in (
            "wt_done", "w_summed", "w_hi_done", "w_lo_done"))
        s_summed, s_hi_done, s_lo_done = sem("s_summed"), sem("s_hi_done"), sem("s_lo_done")
        a_hi_done, a_lo_done = sem("a_hi_done"), sem("a_lo_done")
        b_hi_done, b_cat_done, b_saved = sem("b_hi_done"), sem("b_cat_done"), sem("b_saved")
        x_hi_done, x_lo_done = sem("x_hi_done"), sem("x_lo_done")
        blk_done, bias_done, a_done = sem("blk_done"), sem("bias_done"), sem("a_done")
        x2_done, x2_biased, x2_hi_done, x2_lo_done = (sem(n) for n in (
            "x2_done", "x2_biased", "x2_hi_done", "x2_lo_done"))
        h_done, h_masked, ht_done, ht_hi_done, ht_lo_done = (sem(n) for n in (
            "h_done", "h_masked", "ht_done", "ht_hi_done", "ht_lo_done"))
        out_done = sem("out_done")
        out_moved = [sem(f"out_moved{u}") for u in range(2)]

        def in_pairs(eng, step):
            for u in range(2):
                step(u, u, 0, True)
            with eng.Fori(1, TILES // 2 - 1) as pair:
                for u in range(2):
                    step(2 * pair + u, u, pair, True)
            for u in range(2):
                step(TILES - 2 + u, u, TILES // 2 - 1, False)

        block = ctx.enter_context(nc.Block())

        @block.sync
        def _(sp):
            sp.dma_start(index[:, 0, :], subj.rearrange("(a n) -> a n", a=1)).then_inc(index_in, 16)
            sp.dma_start(index[:, 1, :], slot.rearrange("(a n) -> a n", a=1)).then_inc(index_in, 16)
            for u in range(2):
                sp.dma_start(x_raw[u][:], x_t[u]).then_inc(x_in[u], 16)
            for j in range(PER_TILE):
                sp.dma_start(s_raw[ROWS * j:ROWS * (j + 1)], w0.rearrange("s c d -> c s d")).then_inc(s_in, 16)
            sp.dma_start(bias0[:], b0.rearrange("s a d -> a (s d)").to_broadcast([P, SLOTS * ROWS])).then_inc(bias_in, 16)
            sp.dma_start(a_raw[:], lora_a.rearrange("s (p k) r -> p s (k r)", k=CHUNKS)).then_inc(a_in, 16)
            for q in range(4):
                for part in range(2):
                    at = 32 * q + RANK * part
                    sp.dma_start(b_raw[at:at + RANK], lora_b[8 * q:8 * q + 8].rearrange("s r o -> r s o")).then_inc(b_in, 16)
            for u in range(2):
                sp.wait_ge(x_hi_done, u + 1)
                sp.wait_ge(x_lo_done, u + 1)
                sp.dma_start(x_raw[u][:], x_t[2 + u]).then_inc(x_in[u], 16)
            sp.wait_ge(b_cat_done, 1)
            for q in range(4):
                sp.dma_start(b_split[8 * q:8 * q + 8].rearrange("s e o -> e s o"),
                             b_cat[32 * q:32 * q + 32].bitcast(fp32)).then_inc(b_saved, 16)
            sp.wait_ge(b_saved, 64)
            sp.wait_ge(index_in, 32)

            def take_b(t, u):
                _, slots = nc.values_load_multi_w_load_instructions(
                    index[0:1, 1, bass.ds(t * PER_TILE, PER_TILE)], engines=[mybir.EngineType.SP],
                    min_val=0, max_val=SLOTS - 1, skip_runtime_bounds_check_because="indices name one of the SLOTS")
                for j in range(PER_TILE):
                    sp.dma_start(b_t[u][32 * j:32 * j + 32, :].bitcast(fp32),
                                 b_split[bass.ds(slots[j], 1)].rearrange("a e o -> (a e) o")).then_inc(b_got[u], 16)

            for u in range(2):
                take_b(u, u)

            def step(t, u, pair, ahead):
                if ahead is True:
                    sp.wait_ge(out_done, t + 1)
                    take_b(t + 2, u)
                sp.wait_ge(out_moved[u], pair + 1)
                sp.dma_start(out_t[t] if isinstance(t, int) else out_t[bass.ds(t, 1)].rearrange("a p f -> (a p) f"),
                             out_sb[u][:]).then_inc(stored[u], 16)

            def load_x(t, u):
                sp.wait_ge(x_hi_done, t + 3)
                sp.wait_ge(x_lo_done, t + 3)
                sp.dma_start(x_raw[u][:], x_t[bass.ds(t + 4, 1)].rearrange("a p f -> (a p) f")).then_inc(x_in[u], 16)

            with sp.Fori(0, TILES // 2 - 2) as pair:
                for u in range(2):
                    load_x(2 * pair + u, u)
                    step(2 * pair + u, u, pair, True)
            for u in range(2):
                step(TILES - 4 + u, u, TILES // 2 - 2, True)
            for u in range(2):
                step(TILES - 2 + u, u, TILES // 2 - 1, False)
            for u in range(2):
                sp.wait_ge(stored[u], 16 * (TILES // 2))

        @block.gpsimd
        def _(pool):
            pool.memset(ident[:], 0.0).then_inc(blanks, 1)
            pool.memset(shifted[:], 0.0).then_inc(blanks, 1)
            pool.wait_ge(blanks, 2)
            pool.affine_select(out=ident[:], in_=ident[:], compare_op=ALU.not_equal, fill=1.0, base=0,
                               pattern=[[-1, P]], channel_multiplier=1).then_inc(consts, 1)
            pool.affine_select(out=shifted[:], in_=shifted[:], compare_op=ALU.not_equal, fill=1.0,
                               base=CHUNKS - 1, pattern=[[-1, FEAT + CHUNKS]],
                               channel_multiplier=CHUNKS).then_inc(consts, 1)
            pool.wait_ge(index_in, 32)

            def split_x(t, u, count):
                pool.wait_ge(x_hi_done, t + 1)
                pool.tensor_tensor(x_lo[u][:], x_raw[u][:], x_hi[u][:].bitcast(fp32), ALU.subtract).then_inc(x_lo_done, 1)

            def place_a(t, u):
                _, slots = nc.values_load_multi_w_load_instructions(
                    index[0:1, 1, bass.ds(t * PER_TILE, PER_TILE)], engines=[mybir.EngineType.Pool],
                    min_val=0, max_val=SLOTS - 1, skip_runtime_bounds_check_because="indices name one of the SLOTS")
                for j in range(PER_TILE):
                    at = a_at[u] + RANK * j
                    last = pool.tensor_copy(
                        w_cat[:, :, :, at:at + RANK],
                        a_all[:, bass.ds(slots[j], 1), :, :].rearrange("p a h (k r) -> p (a h) k r", k=CHUNKS))
                last.then_inc(a_done, 1)

            for u in range(2):
                split_x(u, u, u)
            pool.wait_ge(a_hi_done, 1)
            pool.wait_ge(a_lo_done, 1)
            for u in range(2):
                place_a(u, u)

            with pool.Fori(0, TILES // 2 - 1) as pair:
                for u in range(2):
                    t = 2 * pair + u
                    pool.wait_ge(h_done, t + 1)
                    place_a(t + 2, u)
                    split_x(t + 2, u, pair)

        @block.scalar
        def _(act):
            act.dma_start(w_nat[:], w1.rearrange("(c p) f -> p c f", p=P)).then_inc(w_in, 16)
            act.dma_start(bias1[:], b1.rearrange("(a n) -> a n", a=1).to_broadcast([P, FEAT])).then_inc(bias_in, 16)

            def split_x(t, u, pair):
                act.wait_ge(x_in[u], 16 * pair + 16)
                act.copy(x_hi[u][:], x_raw[u][:]).then_inc(x_hi_done, 1)

            def place_w(t, u):
                _, subjects = nc.values_load_multi_w_load_instructions(
                    index[0:1, 0, bass.ds(t * PER_TILE, PER_TILE)], engines=[mybir.EngineType.Activation],
                    min_val=0, max_val=SLOTS - 1, skip_runtime_bounds_check_because="indices name one of the SLOTS")
                for j in range(PER_TILE):
                    rows = slice(ROWS * j, ROWS * (j + 1))
                    last = act.copy(w_blk[u][rows, :, rows],
                                    s_all[rows, bass.ds(subjects[j], 1), :, :].rearrange("p a h d -> p (a h) d"))
                last.then_inc(blk_done, 1)
                for j in range(PER_TILE):
                    last = act.copy(bias_t[u][:, ROWS * j:ROWS * (j + 1)],
                                    bias0[:, bass.ds(subjects[j] * ROWS, ROWS)])
                last.then_inc(bias_done, 1)

            def hi_of_x2(t, u):
                act.wait_ge(x2_biased, t + 1)
                act.copy(x2_hi[u][:], x2_ps[:]).then_inc(x2_hi_done, 1)

            for u in range(2):
                split_x(u, u, 0)
            act.wait_ge(s_summed, 1)
            act.copy(s_all[:, :, 0, :], s_sum[:]).then_inc(s_hi_done, 1)
            for k in range(CHUNKS):
                act.wait_ge(w_summed, k + 1)
                act.copy(w_cat[:, 0, k, :].rearrange("p (g c) -> p g c", g=2)[:, :, 0:HALF],
                         w_sum[:, k, :].rearrange("p (g c) -> p g c", g=2)).then_inc(w_hi_done, 1)
            act.wait_ge(a_in, 16)
            act.copy(a_all[:, :, 0, :], a_raw[:]).then_inc(a_hi_done, 1)
            act.wait_ge(s_lo_done, 1)
            act.wait_ge(s_hi_done, 1)
            act.wait_ge(index_in, 32)
            act.wait_ge(bias_in, 32)
            act.wait_ge(masks, 1)
            for u in range(2):
                place_w(u, u)
            hi_of_x2(0, 0)

            def step(t, u, pair, ahead):
                act.wait_ge(ht_done, t + 1)
                act.copy(ht_hi[:], ht_ps[:]).then_inc(ht_hi_done, 1)
                if ahead or u == 0:
                    hi_of_x2(t + 1, 1 - u)
                if ahead:
                    split_x(t + 2, u, pair + 1)
                    place_w(t + 2, u)

            in_pairs(act, step)

        @block.vector
        def _(dve):
            for u in range(2):
                dve.memset(w_blk[u][:].bitcast(fp32), 0.0)
            dve.memset(h_mask[:], 0.0).then_inc(masks, 1)
            dve.wait_ge(masks, 1)
            for j in range(PER_TILE):
                rows = slice(ROWS * j, ROWS * (j + 1))
                last = dve.memset(h_mask[rows, rows], SCALING)
            last.then_inc(masks, 1)
            dve.wait_ge(consts, 1)
            dve.reduce_sum(eye_rows[:], ident[:].rearrange("p (j d) -> p d j", j=PER_TILE), axis=AX.X).then_inc(masks, 1)
            dve.reduce_sum(lo_half[:], ident[:].rearrange("p (j d) -> p j d", j=PER_TILE)[:, :, RANK:], axis=AX.XY).then_inc(masks, 1)
            dve.wait_ge(masks, 4)
            dve.wait_ge(s_in, 64)
            dve.tensor_tensor(s_sum[:], s_raw[:], eye_rows[:].rearrange("p (a d) -> p a d", a=1).to_broadcast([P, SLOTS, ROWS]),
                              ALU.add).then_inc(s_summed, 1)
            dve.wait_ge(s_hi_done, 1)
            dve.tensor_tensor(s_all[:, :, 1, :], s_sum[:], s_all[:, :, 0, :].bitcast(fp32), ALU.subtract).then_inc(s_lo_done, 1)
            dve.wait_ge(consts, 2)
            for k in range(CHUNKS):
                dve.wait_ge(wt_done, k + 1)
                dve.tensor_tensor(w_sum[:, k, :], wt_ps[k], shifted[:, CHUNKS - 1 - k:CHUNKS - 1 - k + FEAT],
                                  ALU.add).then_inc(w_summed, 1)
            for k in range(CHUNKS):
                dve.wait_ge(w_hi_done, k + 1)
                hi, lo = (w_cat[:, n, k, :].rearrange("p (g c) -> p g c", g=2)[:, :, 0:HALF] for n in range(2))
                dve.tensor_tensor(lo, w_sum[:, k, :].rearrange("p (g c) -> p g c", g=2), hi.bitcast(fp32),
                                  ALU.subtract).then_inc(w_lo_done, 1)
            dve.wait_ge(a_hi_done, 1)
            dve.tensor_tensor(a_all[:, :, 1, :], a_raw[:], a_all[:, :, 0, :].bitcast(fp32), ALU.subtract).then_inc(a_lo_done, 1)

            def bias_x2(t, u):
                dve.wait_ge(x2_done, t + 1)
                dve.wait_ge(bias_done, t + 1)
                dve.tensor_tensor(x2_ps[:], x2_ps[:],
                                  bias_t[u][:].rearrange("p (a d) -> p a d", a=1).to_broadcast([P, CHUNKS, P]),
                                  ALU.add).then_inc(x2_biased, 1)

            def lo_of_x2(t, u):
                dve.wait_ge(x2_hi_done, t + 1)
                dve.tensor_tensor(x2_lo[u][:], x2_ps[:], x2_hi[u][:].bitcast(fp32), ALU.subtract).then_inc(x2_lo_done, 1)

            bias_x2(0, 0)
            lo_of_x2(0, 0)
            dve.wait_ge(b_in, 128)
            dve.tensor_scalar(b_hi[:], b_raw[:], lo_half[:, 0:1], None, ALU.mult).then_inc(b_hi_done, 1)
            dve.wait_ge(b_hi_done, 1)
            dve.tensor_tensor(b_cat[:], b_raw[:], b_hi[:].bitcast(fp32), ALU.subtract).then_inc(b_cat_done, 1)

            def step(t, u, pair, ahead):
                dve.wait_ge(h_done, t + 1)
                h = out_ps[u][:, 1, h_at[u]:h_at[u] + HCOLS].rearrange("p (j a r) -> p j a r", j=PER_TILE, a=1)
                dve.tensor_tensor(h_m[:].rearrange("p (j a r) -> p j a r", j=PER_TILE, a=2),
                                  h.to_broadcast([P, PER_TILE, 2, RANK]),
                                  h_mask[:].rearrange("p (j a r) -> p j a r", j=PER_TILE, a=2),
                                  ALU.mult).then_inc(h_masked, 1)
                if ahead or u == 0:
                    bias_x2(t + 1, 1 - u)
                dve.wait_ge(ht_hi_done, t + 1)
                dve.tensor_tensor(ht_lo[:], ht_ps[:], ht_hi[:].bitcast(fp32), ALU.subtract).then_inc(ht_lo_done, 1)
                if ahead or u == 0:
                    lo_of_x2(t + 1, 1 - u)
                dve.wait_ge(out_done, t + 1)
                if not (isinstance(pair, int) and pair == 0):
                    dve.wait_ge(stored[u], 16 * pair)
                dve.tensor_tensor(out_sb[u][:].rearrange("p (g c) -> p g c", g=2)[:, 0, :], out_ps[u][:, 0, 0:HALF],
                                  bias1[:, 0:HALF], ALU.add)
                dve.tensor_tensor(out_sb[u][:].rearrange("p (g c) -> p g c", g=2)[:, 1, :],
                                  out_ps[u][:, 1, o_at[u]:o_at[u] + HALF],
                                  bias1[:, HALF:], ALU.add).then_inc(out_moved[u], 1)

            in_pairs(dve, step)

        @block.tensor
        def _(pe):
            def parts(out_, left, right, start, stop):
                return pe.matmul(out_, left, right, start=start, stop=stop, skip_group_check=True)

            def to_x2(t, u):
                pe.wait_ge(x_hi_done, t + 1)
                pe.wait_ge(x_lo_done, t + 1)
                pe.wait_ge(blk_done, t + 1)
                for k in range(CHUNKS):
                    xh = x_hi[u][:].rearrange("p (f k) -> p k f", k=CHUNKS)[:, k, :]
                    xl = x_lo[u][:].rearrange("p (f k) -> p k f", k=CHUNKS)[:, k, :]
                    parts(x2_ps[:, k, :], xh, w_blk[u][:, 0, :], True, False)
                    parts(x2_ps[:, k, :], xh, w_blk[u][:, 1, :], False, False)
                    last = parts(x2_ps[:, k, :], xl, w_blk[u][:, 0, :], False, True)
                last.then_inc(x2_done, 1)

            pe.wait_ge(w_in, 16)
            pe.wait_ge(consts, 1)
            for k in range(CHUNKS):
                for c in range(CHUNKS):
                    last = pe.transpose(wt_ps[k][:, P * c:P * (c + 1)],
                                        w_nat[:, c, :].rearrange("p (f k) -> p k f", k=CHUNKS)[:, k, :], ident[:])
                last.then_inc(wt_done, 1)
            to_x2(0, 0)
            pe.wait_ge(w_lo_done, CHUNKS)
            pe.wait_ge(w_summed, CHUNKS)

            def step(t, u, pair, ahead):
                first_out, second_out = out_ps[u][:, 0, 0:HALF], out_ps[u][:, 1, 0:HALF + HCOLS]
                pe.wait_ge(x2_hi_done, t + 1)
                pe.wait_ge(a_done, t + 1)
                if not (isinstance(pair, int) and pair == 0):
                    pe.wait_ge(out_moved[u], pair)
                for k in range(CHUNKS):
                    parts(second_out, x2_hi[u][:, k, :], w_cat[:, 0, k, second[u]], k == 0, False)
                    parts(second_out, x2_hi[u][:, k, :], w_cat[:, 1, k, second[u]], False, False)
                pe.wait_ge(x2_lo_done, t + 1)
                for k in range(CHUNKS):
                    last = parts(second_out, x2_lo[u][:, k, :], w_cat[:, 0, k, second[u]], False, False)
                last.then_inc(h_done, 1)
                if ahead or u == 0:
                    to_x2(t + 1, 1 - u)
                for k in range(CHUNKS):
                    parts(first_out, x2_hi[u][:, k, :], w_cat[:, 0, k, 0:HALF], k == 0, False)
                    parts(first_out, x2_hi[u][:, k, :], w_cat[:, 1, k, 0:HALF], False, False)
                pe.wait_ge(h_masked, t + 1)
                pe.transpose(ht_ps[:], h_m[:], ident[:]).then_inc(ht_done, 1)
                for k in range(CHUNKS):
                    parts(first_out, x2_lo[u][:, k, :], w_cat[:, 0, k, 0:HALF], False, False)
                pe.wait_ge(b_got[u], 64 * (pair + 1))
                pe.wait_ge(ht_hi_done, t + 1)
                halves = [(first_out, b_t[u][:, 0:HALF]),
                          (out_ps[u][:, 1, o_at[u]:o_at[u] + HALF], b_t[u][:, HALF:])]
                for o, b in halves:
                    parts(o, ht_hi[:], b, False, False)
                pe.wait_ge(ht_lo_done, t + 1)
                for o, b in halves:
                    last = parts(o, ht_lo[:], b, False, True)
                last.then_inc(out_done, 1)

            in_pairs(pe, step)

    return nc


_INS = ['x', 'itok_B_0_31', 'itok_B_0_23', 'L0_cond_weights', 'L0_cond_biases', 'L1_cond_W', 'L1_cond_b',
        'L1_cond_lora_As', 'L1_cond_lora_Bs']


def kernel(**inputs):
    import numpy as np
    import concourse.bacc as bacc
    from concourse.bass_utils import run_bass_kernel_spmd

    nc = bacc.Bacc("TRN2", target_bir_lowering=False, num_devices=1)
    arrays, args = {}, []
    for name in _INS:
        a = np.ascontiguousarray(inputs[name])
        arrays[f"in_{name}"] = a
        args.append(nc.dram_tensor(f"in_{name}", a.shape, mybir.dt.from_np(a.dtype), kind="ExternalInput").ap())
    out = nc.dram_tensor("out", (BATCH, ROWS, FEAT), mybir.dt.float32, kind="ExternalOutput").ap()
    build(nc, *args, out)
    result = run_bass_kernel_spmd(nc, [arrays], core_ids=[0])
    return result.results[0]["out"]
```

```python
from contextlib import ExitStack

import concourse.bass as bass
from concourse import mybir

BATCH, ROWS, FEAT = 128, 32, 512
SLOTS, RANK = 32, 16
P = 128
PER_TILE = P // ROWS
TILES = BATCH // PER_TILE
CHUNKS = FEAT // P
HALF = FEAT // 2
HCOLS = PER_TILE * RANK
SCALING = 2.0
WROW = 2 * (HALF + HCOLS)


def build(nc, x, subj, slot, w0, b0, w1, b1, lora_a, lora_b, out):
    fp32 = mybir.dt.float32
    f32r = mybir.dt.float32r
    i32 = mybir.dt.int32
    ALU = mybir.AluOpType
    AX = mybir.AxisListType
    ACT = mybir.ActivationFunctionType

    x_t = x.rearrange("(n b) c f -> n (b c) f", b=PER_TILE)
    out_t = out.rearrange("(n b) c f -> n (b c) f", b=PER_TILE)

    def tile_of(tiles, t):
        return tiles[t] if isinstance(t, int) else tiles[bass.ds(t, 1)].rearrange("a p f -> (a p) f")

    ctx = ExitStack()
    with ctx:
        def sb(name, shape, dt=fp32):
            return ctx.enter_context(nc.sbuf_tensor(name, shape, dt))

        def ps(name, shape):
            return ctx.enter_context(nc.psum_tensor(name, shape, fp32))

        def sem(name):
            return ctx.enter_context(nc.semaphore(name))

        index = sb("index", [1, 2, BATCH], i32)
        subj_row = sb("subj_row", [SLOTS, BATCH], i32)
        subj_f = sb("subj_f", [SLOTS, BATCH])
        number = sb("number", [SLOTS, 1], i32)
        number_f = sb("number_f", [SLOTS, 1])
        one_hot = sb("one_hot", [SLOTS, BATCH])
        b0_rows = sb("b0_rows", [SLOTS, P])
        bias0 = sb("bias0", [P, TILES])
        ident = sb("ident", [P, P])
        eye_rows = sb("eye_rows", [P, ROWS])
        h_mask = sb("h_mask", [P, P])
        w_nat = sb("w_nat", [P, CHUNKS, FEAT])
        w_sum = sb("w_sum", [P, CHUNKS, FEAT])
        w_cat = sb("w_cat", [P, 2, CHUNKS, WROW], f32r)
        bias1 = sb("bias1", [P, FEAT])
        s_raw = sb("s_raw", [P, SLOTS, ROWS])
        s_sum = sb("s_sum", [P, SLOTS, ROWS])
        s_all = sb("s_all", [P, SLOTS, 2, ROWS], f32r)
        a_raw = sb("a_raw", [P, SLOTS, CHUNKS * RANK])
        a_all = sb("a_all", [P, SLOTS, 2, CHUNKS * RANK], f32r)
        lo_rows = sb("lo_rows", [P, 1])

        x_raw = [sb(f"x_raw{u}", [P, FEAT]) for u in range(2)]
        x_hi = [sb(f"x_hi{u}", [P, FEAT], f32r) for u in range(2)]
        x_lo = [sb(f"x_lo{u}", [P, FEAT], f32r) for u in range(2)]
        w_blk = [sb(f"w_blk{u}", [P, 2, P], f32r) for u in range(2)]
        b_raw = [sb(f"b_raw{u}", [P, FEAT]) for u in range(2)]
        b_mid = sb("b_mid", [P, FEAT], f32r)
        b_t = [sb(f"b_t{u}", [P, FEAT], f32r) for u in range(2)]
        x2 = sb("x2", [P, FEAT])
        spare = sb("spare", [P, 1])
        x2t_hi = [sb(f"x2t_hi{u}", [P, CHUNKS, P], f32r) for u in range(2)]
        x2t_lo = [sb(f"x2t_lo{u}", [P, CHUNKS, P], f32r) for u in range(2)]
        h_m = sb("h_m", [P, P])
        ht_hi = sb("ht_hi", [P, P], f32r)
        ht_lo = sb("ht_lo", [P, P], f32r)
        out_sb = [sb(f"out_sb{u}", [P, FEAT]) for u in range(2)]

        x2_ps = ps("x2_ps", [P, FEAT])
        x2t_ps = ps("x2t_ps", [P, CHUNKS, P])
        ht_ps = ps("ht_ps", [P, P])
        out_ps = [ps(f"out_ps{u}", [P, 2, FEAT]) for u in range(2)]
        wt_ps = [out_ps[0][:, 0, :], out_ps[0][:, 1, :], out_ps[1][:, 0, :], out_ps[1][:, 1, :]]

        a_at = [HALF, 2 * HALF + HCOLS]
        second = [slice(HALF, 2 * HALF + HCOLS), slice(HALF + HCOLS, WROW)]
        h_at = [0, HALF]
        o_at = [HCOLS, 0]

        index_in, subj_in, b0_in, b1_in, s_in = (sem(n) for n in (
            "index_in", "subj_in", "b0_in", "b1_in", "s_in"))
        a_in = [sem(f"a_in{n}") for n in range(2)]
        w_in = [sem(f"w_in{c}") for c in range(CHUNKS)]
        x_in = [sem(f"x_in{u}") for u in range(2)]
        b_in = [sem(f"b_in{u}") for u in range(2)]
        stored = [sem(f"stored{u}") for u in range(2)]
        consts, blanks, masks, blocks_zeroed = sem("consts"), sem("blanks"), sem("masks"), sem("blocks_zeroed")
        as_float, one_hot_done, b0_spread, bias0_raw, bias0_done = (sem(n) for n in (
            "as_float", "one_hot_done", "b0_spread", "bias0_raw", "bias0_done"))
        wt_done, w_summed, w_hi_done, w_lo_done = (sem(n) for n in (
            "wt_done", "w_summed", "w_hi_done", "w_lo_done"))
        s_summed, s_hi_done, s_lo_done = sem("s_summed"), sem("s_hi_done"), sem("s_lo_done")
        a_hi_done, a_lo_done = sem("a_hi_done"), sem("a_lo_done")
        b_mid_done, b_done = sem("b_mid_done"), sem("b_done")
        x_hi_done, x_lo_done = sem("x_hi_done"), sem("x_lo_done")
        blk_done, a_done = sem("blk_done"), sem("a_done")
        x2_done, x2_moved, x2t_done, x2t_hi_done, x2t_lo_done = (sem(n) for n in (
            "x2_done", "x2_moved", "x2t_done", "x2t_hi_done", "x2t_lo_done"))
        h_done, h_masked, ht_done, ht_hi_done, ht_lo_done = (sem(n) for n in (
            "h_done", "h_masked", "ht_done", "ht_hi_done", "ht_lo_done"))
        out_done = sem("out_done")
        out_moved = [sem(f"out_moved{u}") for u in range(2)]

        def in_pairs(eng, step):
            pairs = TILES // 2
            for u in range(2):
                step(u, u, 0, TILES)
            with eng.Fori(1, pairs - 3) as pair:
                for u in range(2):
                    step(2 * pair + u, u, pair, TILES)
            for pair in range(pairs - 3, pairs):
                for u in range(2):
                    t = 2 * pair + u
                    step(t, u, pair, TILES - 1 - t)

        def is_first(pair):
            return isinstance(pair, int) and pair == 0

        def four_of(which, t, engine):
            return nc.values_load_multi_w_load_instructions(
                index[0:1, which, bass.ds(t * PER_TILE, PER_TILE)], engines=[engine],
                min_val=0, max_val=SLOTS - 1,
                skip_runtime_bounds_check_because="indices name one of the SLOTS")[1]

        def half_slots(n):
            return slice(SLOTS // 2 * n, SLOTS // 2 * (n + 1))

        def w_block(part, c):
            at = P * c + (HCOLS if c >= CHUNKS // 2 else 0)
            return w_cat[:, part, :, at:at + P]

        def w_sum_block(c):
            return w_sum[:, :, P * c:P * (c + 1)]

        block = ctx.enter_context(nc.Block())

        @block.sync
        def _(sp):
            sp.dma_start(index[:, 0, :], subj.rearrange("(a n) -> a n", a=1)).then_inc(index_in, 16)
            for j in range(PER_TILE):
                sp.dma_start(s_raw[ROWS * j:ROWS * (j + 1)], w0.rearrange("s c d -> c s d")).then_inc(s_in, 16)
            for n in range(2):
                sp.dma_start(a_raw[:, half_slots(n), :],
                             lora_a[half_slots(n)].rearrange("s (p k) r -> p s (k r)", k=CHUNKS)).then_inc(a_in[n], 16)
            sp.dma_start(index[:, 1, :], slot.rearrange("(a n) -> a n", a=1)).then_inc(index_in, 16)
            for c in range(CHUNKS):
                sp.dma_start(w_nat[:, c, :], w1[P * c:P * (c + 1), :]).then_inc(w_in[c], 16)

            def load_x(t, u):
                if not isinstance(t, int) or t >= 2:
                    sp.wait_ge(x_hi_done, t - 1)
                    sp.wait_ge(x_lo_done, t - 1)
                sp.dma_start(x_raw[u][:], tile_of(x_t, t)).then_inc(x_in[u], 16)

            def take_b(t, u):
                slots = four_of(1, t, mybir.EngineType.SP)
                for j in range(PER_TILE):
                    rows = lora_b[bass.ds(slots[j], 1)]
                    sp.dma_start(b_raw[u][32 * j:32 * j + 32, :],
                                 rows.to_broadcast([2, RANK, FEAT])).then_inc(b_in[u], 16)

            sp.wait_ge(index_in, 32)
            take_b(0, 0)
            load_x(2, 0)
            load_x(3, 1)
            take_b(1, 1)
            sp.dma_start(bias1[:], b1.rearrange("(a n) -> a n", a=1).to_broadcast([P, FEAT])).then_inc(b1_in, 16)
            load_x(4, 0)

            def step(t, u, pair, left):
                if left >= 2:
                    sp.wait_ge(b_done, t + 1)
                    take_b(t + 2, u)
                if left >= 5:
                    load_x(t + 5, 1 - u)
                sp.wait_ge(out_moved[u], pair + 1)
                sp.dma_start(tile_of(out_t, t), out_sb[u][:]).then_inc(stored[u], 16)

            in_pairs(sp, step)
            for u in range(2):
                sp.wait_ge(stored[u], 16 * (TILES // 2))

        @block.gpsimd
        def _(pool):
            pool.memset(ident[:], 0.0).then_inc(blanks, 1)
            pool.wait_ge(blanks, 1)
            pool.affine_select(out=ident[:], in_=ident[:], compare_op=ALU.not_equal, fill=1.0, base=0,
                               pattern=[[-1, P]], channel_multiplier=1).then_inc(consts, 1)
            pool.iota(number[:], pattern=[[0, 1]], base=0, channel_multiplier=1).then_inc(consts, 1)
            pool.memset(w_sum[:], 0.0).then_inc(blanks, 1)
            pool.wait_ge(blanks, 2)
            pool.affine_select(out=w_sum[:], in_=w_sum[:], compare_op=ALU.not_equal, fill=1.0, base=0,
                               pattern=[[1, CHUNKS], [-1, FEAT]], channel_multiplier=CHUNKS).then_inc(consts, 1)

            def lo_of_x(t, u):
                pool.wait_ge(x_hi_done, t + 1)
                pool.tensor_tensor(x_lo[u][:], x_raw[u][:], x_hi[u][:].bitcast(fp32), ALU.subtract).then_inc(x_lo_done, 1)

            def place_a(t, u):
                slots = four_of(1, t, mybir.EngineType.Pool)
                for j in range(PER_TILE):
                    at = a_at[u] + RANK * j
                    last = pool.tensor_copy(
                        w_cat[:, :, :, at:at + RANK],
                        a_all[:, bass.ds(slots[j], 1), :, :].rearrange("p a h (k r) -> p (a h) k r", k=CHUNKS))
                last.then_inc(a_done, 1)

            lo_of_x(0, 0)
            lo_of_x(1, 1)
            lo_of_x(2, 0)
            pool.wait_ge(index_in, 32)
            pool.wait_ge(a_hi_done, 2)
            pool.wait_ge(a_lo_done, 2)
            for u in range(2):
                place_a(u, u)

            def step(t, u, pair, left):
                if left >= 3:
                    lo_of_x(t + 3, 1 - u)
                if left >= 2:
                    pool.wait_ge(h_done, t + 1)
                    place_a(t + 2, u)

            in_pairs(pool, step)

        @block.scalar
        def _(act):
            for u in range(2):
                act.dma_start(x_raw[u][:], x_t[u]).then_inc(x_in[u], 16)
                if u == 0:
                    act.dma_start(subj_row[:], subj.rearrange("(a n) -> a n", a=1).to_broadcast([SLOTS, BATCH])).then_inc(subj_in, 16)
                    act.dma_start(b0_rows[:, 0:ROWS], b0.rearrange("s a d -> s (a d)")).then_inc(b0_in, 16)
            act.wait_ge(masks, 2)
            act.copy(spare[:], h_mask[:, 0:1])

            def mid_of_b(t, u, pair):
                act.wait_ge(b_in[u], 16 * PER_TILE * (pair + 1))
                if not isinstance(t, int) or t >= 1:
                    act.wait_ge(b_done, t)
                act.mul(b_mid[:], b_raw[u][:], lo_rows[:, 0:1]).then_inc(b_mid_done, 1)

            def hi_of_x(t, u, pair):
                act.wait_ge(x_in[u], 16 * pair + 16)
                act.copy(x_hi[u][:], x_raw[u][:]).then_inc(x_hi_done, 1)

            def place_w(t, u):
                subjects = four_of(0, t, mybir.EngineType.Activation)
                for j in range(PER_TILE):
                    rows = slice(ROWS * j, ROWS * (j + 1))
                    last = act.copy(w_blk[u][rows, :, rows],
                                    s_all[rows, bass.ds(subjects[j], 1), :, :].rearrange("p a h d -> p (a h) d"))
                last.then_inc(blk_done, 1)

            def move_x2(t, u):
                act.wait_ge(x2_done, t + 1)
                if not isinstance(t, int) or t >= 1:
                    act.wait_ge(x2t_done, t)
                bias = bias0[:, t:t + 1] if isinstance(t, int) else bias0[:, bass.ds(t, 1)]
                act.activation(x2[:], x2_ps[:], ACT.Identity, bias=bias).then_inc(x2_moved, 1)

            def hi_of_x2t(t, u):
                act.wait_ge(x2t_done, t + 1)
                act.copy(x2t_hi[u][:], x2t_ps[:]).then_inc(x2t_hi_done, 1)

            hi_of_x(0, 0, 0)
            act.wait_ge(s_summed, 1)
            act.copy(s_all[:, :, 0, :], s_sum[:]).then_inc(s_hi_done, 1)
            hi_of_x(1, 1, 0)
            act.wait_ge(blocks_zeroed, 1)
            act.wait_ge(index_in, 32)
            act.wait_ge(s_hi_done, 1)
            act.wait_ge(s_lo_done, 1)
            for u in range(2):
                place_w(u, u)
            act.wait_ge(b0_in, 16)
            for j in range(1, PER_TILE):
                last = act.copy(b0_rows[:, ROWS * j:ROWS * (j + 1)], b0_rows[:, 0:ROWS])
            last.then_inc(b0_spread, 1)
            for n in range(2):
                act.wait_ge(a_in[n], 16)
                act.copy(a_all[:, half_slots(n), 0, :], a_raw[:, half_slots(n), :]).then_inc(a_hi_done, 1)
            act.wait_ge(bias0_done, 1)
            move_x2(0, 0)
            hi_of_x(2, 0, 1)
            place_w(2, 0)
            for c in range(CHUNKS):
                act.wait_ge(w_summed, c + 1)
                act.copy(w_block(0, c), w_sum_block(c)).then_inc(w_hi_done, 1)
            hi_of_x2t(0, 0)
            move_x2(1, 1)
            mid_of_b(0, 0, 0)

            def step(t, u, pair, left):
                if left >= 1:
                    hi_of_x2t(t + 1, 1 - u)
                act.wait_ge(ht_done, t + 1)
                act.copy(ht_hi[:], ht_ps[:]).then_inc(ht_hi_done, 1)
                if left >= 2:
                    move_x2(t + 2, u)
                if left >= 1:
                    mid_of_b(t + 1, 1 - u, pair + u)
                if left >= 3:
                    hi_of_x(t + 3, 1 - u, pair + 1 + u)
                    place_w(t + 3, 1 - u)

            in_pairs(act, step)

        @block.vector
        def _(dve):
            for u in range(2):
                last = dve.memset(w_blk[u][:].bitcast(fp32), 0.0)
            last.then_inc(blocks_zeroed, 1)
            dve.memset(h_mask[:], 0.0).then_inc(masks, 1)
            dve.wait_ge(masks, 1)
            for j in range(PER_TILE):
                rows = slice(ROWS * j, ROWS * (j + 1))
                last = dve.memset(h_mask[rows, rows], SCALING)
            last.then_inc(masks, 1)
            dve.wait_ge(consts, 1)
            dve.reduce_sum(eye_rows[:], ident[:].rearrange("p (j d) -> p d j", j=PER_TILE), axis=AX.X).then_inc(masks, 1)
            dve.reduce_sum(lo_rows[:], ident[:].rearrange("p (j d) -> p j d", j=PER_TILE)[:, :, RANK:],
                           axis=AX.XY).then_inc(masks, 1)
            dve.wait_ge(masks, 4)
            dve.wait_ge(s_in, 16 * PER_TILE)
            dve.tensor_tensor(s_sum[:], s_raw[:],
                              eye_rows[:].rearrange("p (a d) -> p a d", a=1).to_broadcast([P, SLOTS, ROWS]),
                              ALU.add).then_inc(s_summed, 1)
            dve.wait_ge(s_hi_done, 1)
            dve.tensor_tensor(s_all[:, :, 1, :], s_sum[:], s_all[:, :, 0, :].bitcast(fp32), ALU.subtract).then_inc(s_lo_done, 1)
            dve.wait_ge(subj_in, 16)
            dve.tensor_copy(subj_f[:], subj_row[:]).then_inc(as_float, 1)
            dve.wait_ge(consts, 2)
            dve.tensor_copy(number_f[:], number[:]).then_inc(as_float, 1)
            dve.wait_ge(as_float, 2)
            dve.tensor_scalar(one_hot[:], subj_f[:], number_f[:, 0:1], None, ALU.is_equal).then_inc(one_hot_done, 1)
            dve.wait_ge(bias0_raw, 1)
            for j in range(PER_TILE):
                rows = slice(ROWS * j, ROWS * (j + 1))
                last = dve.tensor_copy(bias0[rows, :], x2t_ps[rows, 0, :].rearrange("p (t j) -> p j t", j=PER_TILE)[:, j, :])
            last.then_inc(bias0_done, 1)

            for n in range(2):
                slots = half_slots(n)
                dve.wait_ge(a_hi_done, n + 1)
                dve.tensor_tensor(a_all[:, slots, 1, :], a_raw[:, slots, :], a_all[:, slots, 0, :].bitcast(fp32),
                                  ALU.subtract).then_inc(a_lo_done, 1)
            dve.wait_ge(consts, 3)
            for c in range(CHUNKS):
                dve.wait_ge(wt_done, c + 1)
                dve.tensor_tensor(w_sum_block(c), wt_ps[c].rearrange("p (k o) -> p k o", k=CHUNKS), w_sum_block(c),
                                  ALU.add).then_inc(w_summed, 1)
            for c in range(CHUNKS):
                dve.wait_ge(w_hi_done, c + 1)
                dve.tensor_tensor(w_block(1, c), w_sum_block(c), w_block(0, c).bitcast(fp32),
                                  ALU.subtract).then_inc(w_lo_done, 1)

            def lo_of_x2t(t, u):
                dve.wait_ge(x2t_hi_done, t + 1)
                dve.tensor_tensor(x2t_lo[u][:], x2t_ps[:], x2t_hi[u][:].bitcast(fp32), ALU.subtract).then_inc(x2t_lo_done, 1)

            lo_of_x2t(0, 0)

            def parts_of_b(t, u):
                dve.wait_ge(b_mid_done, t + 1)
                dve.tensor_tensor(b_t[u][:], b_raw[u][:], b_mid[:].bitcast(fp32), ALU.subtract).then_inc(b_done, 1)

            parts_of_b(0, 0)
            dve.wait_ge(b1_in, 16)

            def step(t, u, pair, left):
                dve.wait_ge(h_done, t + 1)
                h = out_ps[u][:, 1, h_at[u]:h_at[u] + HCOLS].rearrange("p (j a r) -> p j a r", j=PER_TILE, a=1)
                dve.tensor_tensor(h_m[:].rearrange("p (j a r) -> p j a r", j=PER_TILE, a=2),
                                  h.to_broadcast([P, PER_TILE, 2, RANK]),
                                  h_mask[:].rearrange("p (j a r) -> p j a r", j=PER_TILE, a=2),
                                  ALU.mult).then_inc(h_masked, 1)
                if left >= 1:
                    lo_of_x2t(t + 1, 1 - u)
                dve.wait_ge(ht_hi_done, t + 1)
                dve.tensor_tensor(ht_lo[:], ht_ps[:], ht_hi[:].bitcast(fp32), ALU.subtract).then_inc(ht_lo_done, 1)
                if left >= 1:
                    parts_of_b(t + 1, 1 - u)
                dve.wait_ge(out_done, t + 1)
                if not is_first(pair):
                    dve.wait_ge(stored[u], 16 * pair)
                dve.tensor_tensor(out_sb[u][:, 0:HALF], out_ps[u][:, 0, 0:HALF], bias1[:, 0:HALF], ALU.add)
                dve.tensor_tensor(out_sb[u][:, HALF:], out_ps[u][:, 1, o_at[u]:o_at[u] + HALF],
                                  bias1[:, HALF:], ALU.add).then_inc(out_moved[u], 1)

            in_pairs(dve, step)

        @block.tensor
        def _(pe):
            def part(out_, left, right, start=False, stop=False):
                return pe.matmul(out_, left, right, start=start, stop=stop, skip_group_check=True)

            def to_x2(t, u):
                pe.wait_ge(blk_done, t + 1)
                if not isinstance(t, int) or t >= 1:
                    pe.wait_ge(x2_moved, t)
                pe.wait_ge(x_hi_done, t + 1)
                part(x2_ps[:], w_blk[u][:, 0, :], x_hi[u][:], start=True)
                part(x2_ps[:], w_blk[u][:, 1, :], x_hi[u][:])
                pe.wait_ge(x_lo_done, t + 1)
                part(x2_ps[:], w_blk[u][:, 0, :], x_lo[u][:], stop=True).then_inc(x2_done, 1)

            def turn_x2(t):
                pe.wait_ge(x2_moved, t + 1)
                for k in range(CHUNKS):
                    last = pe.transpose(x2t_ps[:, k, :], x2[:].rearrange("p (f k) -> p k f", k=CHUNKS)[:, k, :], ident[:])
                last.then_inc(x2t_done, 1)

            pe.wait_ge(one_hot_done, 1)
            pe.wait_ge(b0_spread, 1)
            pe.matmul(x2t_ps[:, 0, :], b0_rows[:], one_hot[:], start=True, stop=True).then_inc(bias0_raw, 1)
            to_x2(0, 0)
            for c in range(CHUNKS):
                pe.wait_ge(w_in[c], 16)
                for k in range(CHUNKS):
                    last = pe.transpose(wt_ps[c][:, P * k:P * (k + 1)],
                                        w_nat[:, c, :].rearrange("p (f k) -> p k f", k=CHUNKS)[:, k, :], ident[:])
                last.then_inc(wt_done, 1)
            turn_x2(0)
            to_x2(1, 1)
            pe.wait_ge(w_lo_done, CHUNKS)

            def step(t, u, pair, left):
                first_out, second_out = out_ps[u][:, 0, 0:HALF], out_ps[u][:, 1, 0:HALF + HCOLS]
                pe.wait_ge(x2t_hi_done, t + 1)
                pe.wait_ge(a_done, t + 1)
                if not is_first(pair):
                    pe.wait_ge(out_moved[u], pair)
                for k in range(CHUNKS):
                    part(second_out, x2t_hi[u][:, k, :], w_cat[:, 0, k, second[u]], start=(k == 0))
                    part(second_out, x2t_hi[u][:, k, :], w_cat[:, 1, k, second[u]])
                pe.wait_ge(x2t_lo_done, t + 1)
                for k in range(CHUNKS):
                    last = part(second_out, x2t_lo[u][:, k, :], w_cat[:, 0, k, second[u]])
                last.then_inc(h_done, 1)
                if left >= 1:
                    turn_x2(t + 1)
                pe.wait_ge(h_masked, t + 1)
                pe.transpose(ht_ps[:], h_m[:], ident[:]).then_inc(ht_done, 1)
                if left >= 2:
                    to_x2(t + 2, u)
                for k in range(CHUNKS):
                    part(first_out, x2t_hi[u][:, k, :], w_cat[:, 0, k, 0:HALF], start=(k == 0))
                    part(first_out, x2t_hi[u][:, k, :], w_cat[:, 1, k, 0:HALF])
                for k in range(CHUNKS):
                    part(first_out, x2t_lo[u][:, k, :], w_cat[:, 0, k, 0:HALF])
                halves = [(first_out, b_t[u][:, 0:HALF]),
                          (out_ps[u][:, 1, o_at[u]:o_at[u] + HALF], b_t[u][:, HALF:])]
                pe.wait_ge(b_done, t + 1)
                pe.wait_ge(ht_hi_done, t + 1)
                for o, b in halves:
                    part(o, ht_hi[:], b)
                pe.wait_ge(ht_lo_done, t + 1)
                for o, b in halves:
                    last = part(o, ht_lo[:], b, stop=True)
                last.then_inc(out_done, 1)

            in_pairs(pe, step)

    return nc


_INS = ['x', 'itok_B_0_31', 'itok_B_0_23', 'L0_cond_weights', 'L0_cond_biases', 'L1_cond_W', 'L1_cond_b',
        'L1_cond_lora_As', 'L1_cond_lora_Bs']


def kernel(**inputs):
    import numpy as np
    import concourse.bacc as bacc
    from concourse.bass_utils import run_bass_kernel_spmd

    nc = bacc.Bacc("TRN2", target_bir_lowering=False, num_devices=1)
    arrays, args = {}, []
    for name in _INS:
        a = np.ascontiguousarray(inputs[name])
        arrays[f"in_{name}"] = a
        args.append(nc.dram_tensor(f"in_{name}", a.shape, mybir.dt.from_np(a.dtype), kind="ExternalInput").ap())
    out = nc.dram_tensor("out", (BATCH, ROWS, FEAT), mybir.dt.float32, kind="ExternalOutput").ap()
    build(nc, *args, out)
    result = run_bass_kernel_spmd(nc, [arrays], core_ids=[0])
    return result.results[0]["out"]
```

```python
from contextlib import ExitStack

import concourse.bass as bass
from concourse import mybir

BATCH, ROWS, FEAT = 128, 32, 512
SLOTS, RANK = 32, 16
P = 128
PER_TILE = P // ROWS
TILES = BATCH // PER_TILE
CHUNKS = FEAT // P
HALF = FEAT // 2
HCOLS = PER_TILE * RANK
SCALING = 2.0
ROUND = 4
PARTS = 4
WROW = 2 * (HALF + HCOLS)


def build(nc, x, subj, slot, w0, b0, w1, b1, lora_a, lora_b, out):
    fp32 = mybir.dt.float32
    f32r = mybir.dt.float32r
    i32 = mybir.dt.int32
    ALU = mybir.AluOpType
    AX = mybir.AxisListType

    x_pairs = x.rearrange("(n g b) c f -> n (b c) g f", g=2, b=PER_TILE)
    out_pairs = out.rearrange("(n g b) c f -> n (b c) g f", g=2, b=PER_TILE)

    def pair_of(pairs, n):
        return pairs[n] if isinstance(n, int) else pairs[bass.ds(n, 1)].rearrange("a p g f -> (a p) g f")

    ctx = ExitStack()
    with ctx:
        def sb(name, shape, dt=fp32):
            return ctx.enter_context(nc.sbuf_tensor(name, shape, dt))

        def ps(name, shape):
            return ctx.enter_context(nc.psum_tensor(name, shape, fp32))

        def sem(name):
            return ctx.enter_context(nc.semaphore(name))

        index = sb("index", [1, 2, BATCH], i32)
        ident = sb("ident", [P, P])
        ones = sb("ones", [1, P])
        spread = sb("spread", [ROWS, PER_TILE, ROWS])
        h_mask = sb("h_mask", [P, P])
        lo_rows = sb("lo_rows", [P, 1])
        b0_all = sb("b0_all", [P, SLOTS, ROWS])
        b1_row = sb("b1_row", [1, FEAT])
        bias1 = sb("bias1", [P, FEAT])
        w_nat = sb("w_nat", [P, CHUNKS, FEAT])
        w_cat = sb("w_cat", [P, 2, CHUNKS, WROW], f32r)
        s_raw = sb("s_raw", [ROWS, SLOTS, ROWS])
        s_all = sb("s_all", [P, SLOTS, 2, ROWS], f32r)
        a_raw = sb("a_raw", [P, SLOTS, CHUNKS * RANK])
        a_all = sb("a_all", [P, SLOTS, 2, CHUNKS * RANK], f32r)

        x_raw = [sb(f"x_raw{v}", [P, 2, FEAT]) for v in range(2)]
        x_hi = [sb(f"x_hi{u}", [P, FEAT], f32r) for u in range(2)]
        x_lo = [sb(f"x_lo{u}", [P, FEAT], f32r) for u in range(2)]
        w_blk = [sb(f"w_blk{u}", [P, 2, P], f32r) for u in range(2)]
        b_raw = [sb(f"b_raw{i}", [P, FEAT]) for i in range(ROUND)]
        b_mid = sb("b_mid", [P, FEAT], f32r)
        b_t = [sb(f"b_t{u}", [P, FEAT], f32r) for u in range(2)]
        spare = sb("spare", [P, 1])
        bias0 = [sb(f"bias0{u}", [P, 1, P]) for u in range(2)]
        x2t_begin = sb("x2t_begin", [P, CHUNKS, P])
        x2t = sb("x2t", [P, CHUNKS, P])
        x2t_hi = [sb(f"x2t_hi{u}", [P, CHUNKS, P], f32r) for u in range(2)]
        x2t_lo = [sb(f"x2t_lo{u}", [P, CHUNKS, P], f32r) for u in range(2)]
        h_m = sb("h_m", [P, P])
        ht_hi = sb("ht_hi", [P, P], f32r)
        ht_lo = sb("ht_lo", [P, P], f32r)
        out_sb = [sb(f"out_sb{v}", [P, 2, FEAT]) for v in range(2)]

        x2t_ps = ps("x2t_ps", [P, CHUNKS, 2, P])
        ht_ps = ps("ht_ps", [P, P])
        b1_ps = ps("b1_ps", [P, FEAT])
        out_ps = [ps(f"out_ps{u}", [P, 2, FEAT]) for u in range(2)]
        wt_ps = [out_ps[0][:, 0, :], out_ps[0][:, 1, :], out_ps[1][:, 0, :], out_ps[1][:, 1, :]]
        s_ps = [out_ps[1][:, n, :].rearrange("p (s d) -> p s d", s=SLOTS // 2) for n in range(2)]

        a_at = [HALF, 2 * HALF + HCOLS]
        second = [slice(HALF, 2 * HALF + HCOLS), slice(HALF + HCOLS, WROW)]
        h_at = [0, HALF]
        o_at = [HCOLS, 0]

        subj_in, slot_in, b0_in, b1_in, s_in = (sem(n) for n in (
            "subj_in", "slot_in", "b0_in", "b1_in", "s_in"))
        a_in = [sem(f"a_in{n}") for n in range(PARTS)]
        w_in = [sem(f"w_in{c}") for c in range(CHUNKS)]
        x0_in = sem("x0_in")
        x_in = [sem(f"x_in{v}") for v in range(2)]
        b_in = [sem(f"b_in{i}") for i in range(ROUND)]
        stored = [sem(f"stored{v}") for v in range(2)]
        ident_zeroed, ident_done, ones_done, spread_done = (sem(n) for n in (
            "ident_zeroed", "ident_done", "ones_done", "spread_done"))
        mask_zeroed, masks_done, blocks_zeroed = sem("mask_zeroed"), sem("masks_done"), sem("blocks_zeroed")
        s_summed, s_spread, s_hi_done, s_lo_done = (sem(n) for n in (
            "s_summed", "s_spread", "s_hi_done", "s_lo_done"))
        b1_spread, b1_done = sem("b1_spread"), sem("b1_done")
        w_summed, wt_done, w_hi_done, w_lo_done = (sem(n) for n in (
            "w_summed", "wt_done", "w_hi_done", "w_lo_done"))
        a_hi_done, a_lo_done = sem("a_hi_done"), sem("a_lo_done")
        bias0_done = sem("bias0_done")
        b_mid_done, b_done = sem("b_mid_done"), sem("b_done")
        x_hi_done, x_lo_done = sem("x_hi_done"), sem("x_lo_done")
        blk_done, a_done = sem("blk_done"), sem("a_done")
        x2t_parts, x2t_begun, x2t_summed, x2t_hi_done, x2t_lo_done = (sem(n) for n in (
            "x2t_parts", "x2t_begun", "x2t_summed", "x2t_hi_done", "x2t_lo_done"))
        h_done, h_masked, ht_done, ht_hi_done, ht_lo_done = (sem(n) for n in (
            "h_done", "h_masked", "ht_done", "ht_hi_done", "ht_lo_done"))
        out_done = sem("out_done")
        half_moved = sem("half_moved")
        out_moved = [sem(f"out_moved{u}") for u in range(2)]

        def in_rounds(eng, step):
            rounds = TILES // ROUND
            for i in range(ROUND):
                step(i, i, i // 2, TILES - 1 - i)
            with eng.Fori(1, rounds - 1) as n:
                for i in range(ROUND):
                    step(ROUND * n + i, i, ROUND // 2 * n + i // 2, ROUND + 1)
            for i in range(ROUND):
                t = TILES - ROUND + i
                step(t, i, t // 2, ROUND - 1 - i)

        def peeled(t):
            return isinstance(t, int)

        def rounds_of(pair, v):
            return pair // 2 + 1 if isinstance(pair, int) else (pair - v) // 2 + 1

        def four_of(which, t, engine):
            return nc.values_load_multi_w_load_instructions(
                index[0:1, which, bass.ds(t * PER_TILE, PER_TILE)], engines=[engine],
                min_val=0, max_val=SLOTS - 1,
                skip_runtime_bounds_check_because="indices name one of the SLOTS")[1]

        def slots_of(n, parts):
            return slice(SLOTS // parts * n, SLOTS // parts * (n + 1))

        def w_block(part, c):
            at = P * c + (HCOLS if c >= CHUNKS // 2 else 0)
            return w_cat[:, part, :, at:at + P]

        def wt_block(c):
            return wt_ps[c].rearrange("p (k o) -> p k o", k=CHUNKS)

        def lo_of_a(eng, n):
            slots = slots_of(n, PARTS)
            eng.wait_ge(a_hi_done, n + 1)
            eng.tensor_tensor(a_all[:, slots, 1, :], a_raw[:, slots, :], a_all[:, slots, 0, :].bitcast(fp32),
                              ALU.subtract).then_inc(a_lo_done, 1)

        block = ctx.enter_context(nc.Block())

        @block.sync
        def _(sp):
            sp.dma_start(s_raw[:], w0.rearrange("s c d -> c s d")).then_inc(s_in, 16)
            sp.dma_start(index[:, 0, :], subj.rearrange("(a n) -> a n", a=1)).then_inc(subj_in, 16)
            for c in range(CHUNKS):
                sp.dma_start(w_nat[:, c, :], w1[P * c:P * (c + 1), :]).then_inc(w_in[c], 16)
            sp.dma_start(index[:, 1, :], slot.rearrange("(a n) -> a n", a=1)).then_inc(slot_in, 16)
            for n in range(PARTS):
                sp.dma_start(a_raw[:, slots_of(n, PARTS), :],
                             lora_a[slots_of(n, PARTS)].rearrange("s (p k) r -> p s (k r)", k=CHUNKS)).then_inc(a_in[n], 16)

            def load_x(pair, v):
                if not isinstance(pair, int) or pair >= 2:
                    sp.wait_ge(x_hi_done, 2 * pair - 2)
                    sp.wait_ge(x_lo_done, 2 * pair - 2)
                sp.dma_start(x_raw[v][:], pair_of(x_pairs, pair)).then_inc(x_in[v], 16)

            def take_b(t, i):
                slots = four_of(1, t, mybir.EngineType.SP)
                for j in range(PER_TILE):
                    rows = lora_b[bass.ds(slots[j], 1)]
                    sp.dma_start(b_raw[i][32 * j:32 * j + 32, :],
                                 rows.to_broadcast([2, RANK, FEAT])).then_inc(b_in[i], 16)

            load_x(1, 1)
            sp.wait_ge(slot_in, 16)
            for i in range(ROUND - 1):
                take_b(i, i)

            def step(t, i, pair, left):
                if left >= 5 and i % 2 == 0:
                    load_x(pair + 2, i // 2)
                if left >= ROUND - 1:
                    if not peeled(t) or t >= 1:
                        sp.wait_ge(b_done, t)
                    take_b(t + ROUND - 1, (i + ROUND - 1) % ROUND)

            in_rounds(sp, step)
            sp.wait_ge(stored[0], 16 * (TILES // ROUND))
            sp.wait_ge(stored[1], 16 * (TILES // ROUND + 2))

        @block.gpsimd
        def _(pool):
            pool.memset(ident[:], 0.0).then_inc(ident_zeroed, 1)
            pool.wait_ge(ident_zeroed, 1)
            pool.affine_select(out=ident[:], in_=ident[:], compare_op=ALU.not_equal, fill=1.0, base=0,
                               pattern=[[-1, P]], channel_multiplier=1).then_inc(ident_done, 1)
            pool.wait_ge(ident_done, 1)

            def lo_of_x(t, i):
                u = i % 2
                pool.wait_ge(x_hi_done, t + 1)
                pool.tensor_tensor(x_lo[u][:], x_raw[i // 2][:, u, :], x_hi[u][:].bitcast(fp32), ALU.subtract).then_inc(x_lo_done, 1)

            def place_b0(t, u):
                subjects = four_of(0, t, mybir.EngineType.Pool)
                if not peeled(t) or t >= 2:
                    pool.wait_ge(x2t_summed, t - 1)
                for j in range(PER_TILE):
                    last = pool.tensor_copy(bias0[u][:, :, ROWS * j:ROWS * (j + 1)], b0_all[:, bass.ds(subjects[j], 1), :])
                last.then_inc(bias0_done, 1)

            def parts_of_b(t, i):
                u = i % 2
                pool.wait_ge(b_mid_done, t + 1)
                if not peeled(t) or t >= 2:
                    pool.wait_ge(out_done, t - 1)
                pool.tensor_tensor(b_t[u][:], b_raw[i][:], b_mid[:].bitcast(fp32), ALU.subtract).then_inc(b_done, 1)

            for c in range(CHUNKS):
                if c == 1:
                    lo_of_x(0, 0)
                diagonal = w_nat[:, c, P * c:P * (c + 1)]
                pool.wait_ge(w_in[c], 16)
                pool.tensor_tensor(diagonal, diagonal, ident[:], ALU.add).then_inc(w_summed, 1)
            lo_of_x(1, 1)
            pool.wait_ge(subj_in, 16)
            pool.wait_ge(b0_in, 16)
            for u in range(2):
                place_b0(u, u)
            for n in range(2):
                lo_of_a(pool, n)
            place_b0(2, 0)
            lo_of_x(2, 2)
            parts_of_b(0, 0)

            def step(t, i, pair, left):
                u = i % 2
                if left >= 3:
                    lo_of_x(t + 3, (i + 3) % ROUND)
                    place_b0(t + 3, 1 - u)
                if left >= 1:
                    parts_of_b(t + 1, (i + 1) % ROUND)

            in_rounds(pool, step)

        @block.scalar
        def _(act):
            act.dma_start(x_raw[0][:, 0, :], x_pairs[0][:, 0, :]).then_inc(x0_in, 16)
            act.dma_start(x_raw[0][:, 1, :], x_pairs[0][:, 1, :]).then_inc(x_in[0], 16)
            act.dma_start(b0_all[:], b0.rearrange("s a d -> a s d").to_broadcast([P, SLOTS, ROWS])).then_inc(b0_in, 16)
            act.dma_start(b1_row[:], b1.rearrange("(a n) -> a n", a=1)).then_inc(b1_in, 16)
            act.wait_ge(ones_done, 1)
            act.copy(spare[0:1, :], ones[:, 0:1])

            def mid_of_b(t, i, pair):
                act.wait_ge(b_in[i], 16 * PER_TILE * rounds_of(pair, i // 2))
                if not peeled(t) or t >= 1:
                    act.wait_ge(b_done, t)
                act.mul(b_mid[:], b_raw[i][:], lo_rows[:, 0:1]).then_inc(b_mid_done, 1)

            def hi_of_x(t, i, pair):
                u, v = i % 2, i // 2
                if peeled(t) and t == 0:
                    act.wait_ge(x0_in, 16)
                else:
                    act.wait_ge(x_in[v], 16 * rounds_of(pair, v))
                if not peeled(t) or t >= 2:
                    act.wait_ge(x2t_parts, t - 1)
                act.copy(x_hi[u][:], x_raw[v][:, u, :]).then_inc(x_hi_done, 1)

            def place_a(t, u):
                slots = four_of(1, t, mybir.EngineType.Activation)
                if peeled(t) and t < 2:
                    act.wait_ge(a_hi_done, PARTS)
                    act.wait_ge(a_lo_done, PARTS)
                else:
                    act.wait_ge(h_done, t - 1)
                for j in range(PER_TILE):
                    at = a_at[u] + RANK * j
                    last = act.copy(
                        w_cat[:, :, :, at:at + RANK],
                        a_all[:, bass.ds(slots[j], 1), :, :].rearrange("p a h (k r) -> p (a h) k r", k=CHUNKS))
                last.then_inc(a_done, 1)

            def hi_of_x2t(t, u):
                act.wait_ge(x2t_summed, t + 1)
                if not peeled(t) or t >= 2:
                    act.wait_ge(out_done, t - 1)
                act.copy(x2t_hi[u][:], x2t[:]).then_inc(x2t_hi_done, 1)

            def hi_of_w(c):
                act.wait_ge(wt_done, c + 1)
                act.copy(w_block(0, c), wt_block(c)).then_inc(w_hi_done, 1)

            def hi_of_a(n):
                act.wait_ge(a_in[n], 16)
                act.copy(a_all[:, slots_of(n, PARTS), 0, :], a_raw[:, slots_of(n, PARTS), :]).then_inc(a_hi_done, 1)

            hi_of_x(0, 0, 0)
            for n in range(2):
                act.wait_ge(s_spread, n + 1)
                act.copy(s_all[:, slots_of(n, 2), 0, :], s_ps[n]).then_inc(s_hi_done, 1)
            hi_of_x(1, 1, 0)
            for c in range(CHUNKS):
                hi_of_w(c)
            hi_of_a(0)
            hi_of_a(1)
            act.wait_ge(b1_spread, 1)
            act.copy(bias1[:], b1_ps[:]).then_inc(b1_done, 1)
            hi_of_a(2)
            hi_of_x2t(0, 0)
            hi_of_a(3)
            act.wait_ge(slot_in, 16)
            place_a(0, 0)
            hi_of_x(2, 2, 1)
            act.wait_ge(masks_done, 2)
            mid_of_b(0, 0, 0)
            place_a(1, 1)

            def store(pair, v):
                for u in range(2):
                    act.wait_ge(out_moved[u], pair + 1)
                act.dma_start(pair_of(out_pairs, pair), out_sb[v][:]).then_inc(stored[v], 16)

            def store_alone(t, i, columns, is_moved, count):
                act.wait_ge(is_moved, count)
                act.dma_start(out_pairs[t // 2][:, i % 2, columns], out_sb[i // 2][:, i % 2, columns]).then_inc(stored[i // 2], 16)

            def step(t, i, pair, left):
                u = i % 2
                if left >= 1:
                    hi_of_x2t(t + 1, 1 - u)
                if left >= 3:
                    hi_of_x(t + 3, (i + 3) % ROUND, pair + 1 + u)
                if left >= 1 and not (peeled(t) and t == 0):
                    mid_of_b(t + 1, (i + 1) % ROUND, pair + u)
                if u == 0 and (not peeled(t) or t >= 2):
                    store(pair - 1, 1 - i // 2)
                if left == 0:
                    store_alone(t - 1, i - 1, slice(0, FEAT), out_moved[0], TILES // 2)
                act.wait_ge(ht_done, t + 1)
                act.copy(ht_hi[:], ht_ps[:]).then_inc(ht_hi_done, 1)
                if peeled(t) and t == 0:
                    mid_of_b(1, 1, 0)
                if left >= 2:
                    place_a(t + 2, u)

            in_rounds(act, step)
            store_alone(TILES - 1, ROUND - 1, slice(0, HALF), half_moved, 1)
            store_alone(TILES - 1, ROUND - 1, slice(HALF, FEAT), out_moved[1], TILES // 2)

        @block.vector
        def _(dve):
            dve.memset(ones[:], 1.0).then_inc(ones_done, 1)
            for u in range(2):
                last = dve.memset(w_blk[u][:].bitcast(fp32), 0.0)
            last.then_inc(blocks_zeroed, 1)
            dve.memset(h_mask[:], 0.0).then_inc(mask_zeroed, 1)
            dve.wait_ge(mask_zeroed, 1)
            for j in range(PER_TILE):
                rows = slice(ROWS * j, ROWS * (j + 1))
                last = dve.memset(h_mask[rows, rows], SCALING)
            last.then_inc(masks_done, 1)
            dve.wait_ge(ident_done, 1)
            eye = ident[0:ROWS, 0:ROWS].rearrange("p (a d) -> p a d", a=1)
            dve.tensor_copy(spread[:], eye.to_broadcast([ROWS, PER_TILE, ROWS])).then_inc(spread_done, 1)
            dve.reduce_sum(lo_rows[:], ident[:].rearrange("p (j d) -> p j d", j=PER_TILE)[:, :, RANK:],
                           axis=AX.XY).then_inc(masks_done, 1)
            dve.wait_ge(s_in, 16)
            for n in range(2):
                slots = s_raw[:, slots_of(n, 2), :]
                dve.tensor_tensor(slots, slots, eye.to_broadcast([ROWS, SLOTS // 2, ROWS]), ALU.add).then_inc(s_summed, 1)
            for n in range(2):
                dve.wait_ge(s_hi_done, n + 1)
                dve.tensor_tensor(s_all[:, slots_of(n, 2), 1, :], s_ps[n], s_all[:, slots_of(n, 2), 0, :].bitcast(fp32),
                                  ALU.subtract).then_inc(s_lo_done, 1)

            def lo_of_w(c):
                dve.wait_ge(w_hi_done, c + 1)
                dve.tensor_tensor(w_block(1, c), wt_block(c), w_block(0, c).bitcast(fp32),
                                  ALU.subtract).then_inc(w_lo_done, 1)

            def begin_x2t(t, u):
                dve.wait_ge(x2t_parts, t + 1)
                dve.wait_ge(bias0_done, t + 1)
                if not peeled(t) or t >= 1:
                    dve.wait_ge(x2t_summed, t)
                dve.tensor_tensor(x2t_begin[:], x2t_ps[:, :, 1, :], bias0[u][:].to_broadcast([P, CHUNKS, P]),
                                  ALU.add).then_inc(x2t_begun, 1)

            def sum_x2t(t):
                dve.wait_ge(x2t_begun, t + 1)
                if not peeled(t) or t >= 1:
                    dve.wait_ge(x2t_lo_done, t)
                dve.tensor_tensor(x2t[:], x2t_ps[:, :, 0, :], x2t_begin[:], ALU.add).then_inc(x2t_summed, 1)

            def lo_of_x2t(t, u):
                dve.wait_ge(x2t_hi_done, t + 1)
                dve.tensor_tensor(x2t_lo[u][:], x2t[:], x2t_hi[u][:].bitcast(fp32), ALU.subtract).then_inc(x2t_lo_done, 1)

            def place_w(t, u):
                subjects = four_of(0, t, mybir.EngineType.DVE)
                if not peeled(t) or t >= 2:
                    dve.wait_ge(x2t_parts, t - 1)
                for j in range(PER_TILE):
                    rows = slice(ROWS * j, ROWS * (j + 1))
                    last = dve.tensor_copy(w_blk[u][rows, :, rows],
                                           s_all[rows, bass.ds(subjects[j], 1), :, :].rearrange("p a h d -> p (a h) d"))
                last.then_inc(blk_done, 1)

            dve.wait_ge(subj_in, 16)
            dve.wait_ge(blocks_zeroed, 1)
            dve.wait_ge(s_hi_done, 2)
            dve.wait_ge(s_lo_done, 2)
            place_w(0, 0)
            for c in range(CHUNKS - 1):
                lo_of_w(c)
            begin_x2t(0, 0)
            lo_of_w(CHUNKS - 1)
            sum_x2t(0)
            place_w(1, 1)
            lo_of_a(dve, 2)
            lo_of_x2t(0, 0)
            lo_of_a(dve, 3)
            begin_x2t(1, 1)
            sum_x2t(1)
            place_w(2, 0)
            dve.wait_ge(b1_done, 1)

            def step(t, i, pair, left):
                u, v = i % 2, i // 2
                dve.wait_ge(h_done, t + 1)
                h = out_ps[u][:, 1, h_at[u]:h_at[u] + HCOLS].rearrange("p (j a r) -> p j a r", j=PER_TILE, a=1)
                dve.tensor_tensor(h_m[:].rearrange("p (j a r) -> p j a r", j=PER_TILE, a=2),
                                  h.to_broadcast([P, PER_TILE, 2, RANK]),
                                  h_mask[:].rearrange("p (j a r) -> p j a r", j=PER_TILE, a=2),
                                  ALU.mult).then_inc(h_masked, 1)
                if left >= 1:
                    lo_of_x2t(t + 1, 1 - u)
                if left >= 2:
                    begin_x2t(t + 2, u)
                dve.wait_ge(ht_hi_done, t + 1)
                dve.tensor_tensor(ht_lo[:], ht_ps[:], ht_hi[:].bitcast(fp32), ALU.subtract).then_inc(ht_lo_done, 1)
                if left >= 2:
                    sum_x2t(t + 2)
                if left >= 3:
                    place_w(t + 3, 1 - u)
                dve.wait_ge(out_done, t + 1)
                if not peeled(t) or t >= ROUND:
                    dve.wait_ge(stored[v], 16 * (rounds_of(pair, v) - 1))
                first = dve.tensor_tensor(out_sb[v][:, u, 0:HALF], out_ps[u][:, 0, 0:HALF], bias1[:, 0:HALF], ALU.add)
                if left == 0:
                    first.then_inc(half_moved, 1)
                dve.tensor_tensor(out_sb[v][:, u, HALF:], out_ps[u][:, 1, o_at[u]:o_at[u] + HALF],
                                  bias1[:, HALF:], ALU.add).then_inc(out_moved[u], 1)

            in_rounds(dve, step)

        @block.tensor
        def _(pe):
            def part(out_, left, right, start=False, stop=False):
                return pe.matmul(out_, left, right, start=start, stop=stop, skip_group_check=True)

            def to_x2t(t, u):
                pe.wait_ge(blk_done, t + 1)
                if not peeled(t) or t >= 1:
                    pe.wait_ge(x2t_summed, t)
                for n, (x_part, is_there) in enumerate(((x_hi[u], x_hi_done), (x_lo[u], x_lo_done))):
                    pe.wait_ge(is_there, t + 1)
                    for k in range(CHUNKS):
                        last = part(x2t_ps[:, k, :, :], x_part[:].rearrange("p (f k) -> p k f", k=CHUNKS)[:, k, :],
                                    w_blk[u][:], start=(n == 0 and k % 2 == 0), stop=(n == 1))
                last.then_inc(x2t_parts, 1)

            def turn_w(c):
                pe.wait_ge(w_summed, c + 1)
                for k in range(CHUNKS):
                    last = pe.transpose(wt_ps[c][:, P * k:P * (k + 1)],
                                        w_nat[:, c, :].rearrange("p (f k) -> p k f", k=CHUNKS)[:, k, :], ident[:])
                last.then_inc(wt_done, 1)

            pe.wait_ge(spread_done, 1)
            for n in range(2):
                pe.wait_ge(s_summed, n + 1)
                pe.matmul(s_ps[n], spread[:].rearrange("c j d -> c (j d)"), s_raw[:, slots_of(n, 2), :],
                          start=True, stop=True).then_inc(s_spread, 1)
            turn_w(0)
            turn_w(1)
            pe.wait_ge(s_lo_done, 2)
            turn_w(2)
            turn_w(3)
            to_x2t(0, 0)
            pe.wait_ge(ones_done, 1)
            pe.wait_ge(b1_in, 16)
            pe.matmul(b1_ps[:], ones[:], b1_row[:], start=True, stop=True).then_inc(b1_spread, 1)
            to_x2t(1, 1)
            pe.wait_ge(w_lo_done, CHUNKS)

            def second_half(t, u, pair):
                o = out_ps[u][:, 1, 0:HALF + HCOLS]
                pe.wait_ge(x2t_hi_done, t + 1)
                pe.wait_ge(a_done, t + 1)
                if not peeled(t) or t >= 2:
                    pe.wait_ge(out_moved[u], pair)
                for k in range(CHUNKS):
                    part(o, x2t_hi[u][:, k, :], w_cat[:, 0, k, second[u]], start=(k == 0))
                    part(o, x2t_hi[u][:, k, :], w_cat[:, 1, k, second[u]])
                pe.wait_ge(x2t_lo_done, t + 1)
                for k in range(CHUNKS):
                    last = part(o, x2t_lo[u][:, k, :], w_cat[:, 0, k, second[u]])
                last.then_inc(h_done, 1)

            def first_half(u, chunks):
                o = out_ps[u][:, 0, 0:HALF]
                for k in chunks:
                    part(o, x2t_hi[u][:, k, :], w_cat[:, 0, k, 0:HALF], start=(k == 0))
                    part(o, x2t_hi[u][:, k, :], w_cat[:, 1, k, 0:HALF])
                    part(o, x2t_lo[u][:, k, :], w_cat[:, 0, k, 0:HALF])

            def turn_h(t):
                pe.wait_ge(h_masked, t + 1)
                pe.transpose(ht_ps[:], h_m[:], ident[:]).then_inc(ht_done, 1)

            def add_h_by_b(t, u):
                halves = [(out_ps[u][:, 0, 0:HALF], b_t[u][:, 0:HALF]),
                          (out_ps[u][:, 1, o_at[u]:o_at[u] + HALF], b_t[u][:, HALF:])]
                pe.wait_ge(b_done, t + 1)
                pe.wait_ge(ht_hi_done, t + 1)
                for o, b in halves:
                    part(o, ht_hi[:], b)
                pe.wait_ge(ht_lo_done, t + 1)
                for o, b in halves:
                    last = part(o, ht_lo[:], b, stop=True)
                last.then_inc(out_done, 1)

            def step(t, i, pair, left):
                u = i % 2
                if peeled(t) and t == 0:
                    pe.wait_ge(x2t_hi_done, 1)
                    pe.wait_ge(x2t_lo_done, 1)
                    first_half(0, range(CHUNKS))
                    second_half(0, 0, 0)
                    to_x2t(2, 0)
                    turn_h(0)
                    add_h_by_b(0, 0)
                elif left >= 2:
                    second_half(t, u, pair)
                    to_x2t(t + 2, u)
                    turn_h(t)
                    first_half(u, range(CHUNKS))
                    add_h_by_b(t, u)
                else:
                    second_half(t, u, pair)
                    first_half(u, range(2))
                    turn_h(t)
                    first_half(u, range(2, CHUNKS))
                    add_h_by_b(t, u)

            in_rounds(pe, step)

    return nc


_INS = ['x', 'itok_B_0_31', 'itok_B_0_23', 'L0_cond_weights', 'L0_cond_biases', 'L1_cond_W', 'L1_cond_b',
        'L1_cond_lora_As', 'L1_cond_lora_Bs']


def kernel(**inputs):
    import numpy as np
    import concourse.bacc as bacc
    from concourse.bass_utils import run_bass_kernel_spmd

    nc = bacc.Bacc("TRN2", target_bir_lowering=False, num_devices=1)
    arrays, args = {}, []
    for name in _INS:
        a = np.ascontiguousarray(inputs[name])
        arrays[f"in_{name}"] = a
        args.append(nc.dram_tensor(f"in_{name}", a.shape, mybir.dt.from_np(a.dtype), kind="ExternalInput").ap())
    out = nc.dram_tensor("out", (BATCH, ROWS, FEAT), mybir.dt.float32, kind="ExternalOutput").ap()
    build(nc, *args, out)
    result = run_bass_kernel_spmd(nc, [arrays], core_ids=[0])
    return result.results[0]["out"]
```
